# Optimizing a Trainium2 kernel written in Bass

```python
import numpy as np
import jax
import jax.numpy as jnp

def _softmax(x, axis=-1):
    return jax.nn.softmax(x, axis=axis)

def _gelu(x):
    return jax.nn.gelu(x, approximate=True)

def _silu(x):
    return jax.nn.silu(x)

def _sigmoid(x):
    return jax.nn.sigmoid(x)

def _layernorm(x, axis=-1, eps=1e-05):
    m = jnp.mean(x, axis=axis, keepdims=True)
    v = jnp.var(x, axis=axis, keepdims=True)
    return (x - m) / jnp.sqrt(v + eps)

def _scatter_add(tgt, idx, src, axis=0):
    return tgt.at[idx].add(src)

def _segment_sum(src, seg, n):
    return jax.ops.segment_sum(src, seg, n)
kernel_name = 'mk_seq_preln_d2_jaxref_r8_834ee7'

def setup_inputs(seed: int=0):
    np.random.seed(seed)
    _w = jnp.asarray

    def _L0_attn_setup():
        import math
        import jax, jax.numpy as jnp
        import numpy as np
        N_HEADS = 16
        THETA = 10000.0

        def _rope_cos_sin(S, head_dim):
            half = head_dim // 2
            inv_freq = 1.0 / THETA ** (jnp.arange(half, dtype=jnp.float32) / half)
            t = jnp.arange(S, dtype=jnp.float32)
            freqs = t[:, None] * inv_freq[None, :]
            return (jnp.cos(freqs), jnp.sin(freqs))

        def _apply_rope(x, cos, sin):
            half = x.shape[-1] // 2
            x1, x2 = (x[..., :half], x[..., half:])
            c = cos[None, None, :, :]
            s = sin[None, None, :, :]
            return jnp.concatenate([x1 * c - x2 * s, x1 * s + x2 * c], axis=-1)
        key = jax.random.key(seed)
        k1, k2, k3 = jax.random.split(key, 3)
        B, S, D = (4, 256, 128)
        x = jax.random.normal(k1, (B, S, D), dtype=jnp.float32)
        w_qkv = jax.random.normal(k2, (3 * D, D), dtype=jnp.float32) * (1.0 / math.sqrt(D))
        w_out = jax.random.normal(k3, (D, D), dtype=jnp.float32) * (1.0 / math.sqrt(D))
        return {'x': x, 'w_qkv': w_qkv, 'w_out': w_out}
    _L0_attn_in = _L0_attn_setup()

    def _L0_ffn_setup():
        import jax, jax.numpy as jnp
        import numpy as np
        D_IN, D_HID = (128, 512)

        def _ternary(key, shape):
            return jax.random.randint(key, shape, -1, 2).astype(jnp.float32)

        def _tlin(x, w, s):
            return jnp.einsum('bsi,oi->bso', x, w) * s
        key = jax.random.key(seed)
        ks = jax.random.split(key, 12)
        inv = lambda fan: 1.0 / np.sqrt(fan).astype(np.float32)
        return {'x': jax.random.normal(ks[0], (4, 256, D_IN), dtype=jnp.float32), 'w1_w': _ternary(ks[1], (D_HID, D_IN)), 'w1_s': jax.random.uniform(ks[2], (D_HID,), dtype=jnp.float32) * inv(D_IN), 'w2_w': _ternary(ks[3], (D_HID, D_IN)), 'w2_s': jax.random.uniform(ks[4], (D_HID,), dtype=jnp.float32) * inv(D_IN), 'h1_w': _ternary(ks[5], (D_HID, D_HID)), 'h1_s': jax.random.uniform(ks[6], (D_HID,), dtype=jnp.float32) * inv(D_HID), 'h2_w': _ternary(ks[7], (D_HID, D_HID)), 'h2_s': jax.random.uniform(ks[8], (D_HID,), dtype=jnp.float32) * inv(D_HID), 'w3_w': _ternary(ks[9], (D_IN, D_HID)), 'w3_s': jax.random.uniform(ks[10], (D_IN,), dtype=jnp.float32) * inv(D_HID)}
    _L0_ffn_in = _L0_ffn_setup()

    def _L1_attn_setup():
        import jax, jax.numpy as jnp
        import numpy as np
        NUM_HEAD = 16
        D_Q = 64
        D_KV = 64
        ROPE_BASE = 10000.0

        def _cos_sin(seq_len, dim):
            pos = jnp.arange(seq_len, dtype=jnp.float32)[:, None]
            ids = jnp.arange(dim // 2, dtype=jnp.float32)
            theta = ROPE_BASE ** (-2.0 * ids) / (dim // 2)
            r = pos * theta[None, :]
            return (jnp.cos(r), jnp.sin(r))

        def _rope(x, cos, sin):
            b, s, d = x.shape
            xv = x.reshape(b, s, d // 2, 2)
            x0, x1 = (xv[..., 0], xv[..., 1])
            out = jnp.stack([x0 * cos - x1 * sin, x1 * cos + x0 * sin], axis=-1)
            return out.reshape(b, s, d)
        key = jax.random.key(seed)
        ks = jax.random.split(key, 10)
        d_model, d_q, d_kv = (128, D_Q, D_KV)
        b, s = (2, 256)
        w = lambda k, i, o: jax.random.normal(k, (i, o), dtype=jnp.float32) * 0.02
        return {'x': jax.random.normal(ks[0], (b, s, d_model), dtype=jnp.float32), 'Wd_q_w': w(ks[1], d_model, d_q), 'Wd_q_b': jnp.zeros((d_q,), jnp.float32), 'Wu_q_w': w(ks[2], d_q, d_model), 'Wu_q_b': jnp.zeros((d_model,), jnp.float32), 'Wq_r_w': w(ks[3], d_q, d_model), 'Wq_r_b': jnp.zeros((d_model,), jnp.float32), 'Wk_r_w': w(ks[4], d_model, d_model), 'Wk_r_b': jnp.zeros((d_model,), jnp.float32), 'Wd_kv_w': w(ks[5], d_model, d_kv), 'Wd_kv_b': jnp.zeros((d_kv,), jnp.float32), 'Wu_k_w': w(ks[6], d_kv, d_model), 'Wu_k_b': jnp.zeros((d_model,), jnp.float32), 'Wu_v_w': w(ks[7], d_kv, d_model), 'Wu_v_b': jnp.zeros((d_model,), jnp.float32), 'Wo_w': w(ks[8], d_model, d_model), 'Wo_b': jnp.zeros((d_model,), jnp.float32)}
    _L1_attn_in = _L1_attn_setup()

    def _L1_ffn_setup():
        import jax, jax.numpy as jnp
        import numpy as np
        NUM_EXPERTS = 8
        TOP_K = 2
        D = 128
        H = 4 * D
        B, S = (4, 256)
        key = jax.random.key(seed)
        ks = jax.random.split(key, 8)
        s = 0.02
        return {'x': jax.random.normal(ks[0], (B, S, D), dtype=jnp.float32), 'gate_w': jax.random.normal(ks[1], (NUM_EXPERTS, D), dtype=jnp.float32) * s, 'gate_b': jnp.zeros((NUM_EXPERTS,), dtype=jnp.float32), 'w1': jax.random.normal(ks[2], (NUM_EXPERTS, D, H), dtype=jnp.float32) * s, 'b1': jnp.zeros((NUM_EXPERTS, H), dtype=jnp.float32), 'w2': jax.random.normal(ks[3], (NUM_EXPERTS, H, D), dtype=jnp.float32) * s, 'b2': jnp.zeros((NUM_EXPERTS, D), dtype=jnp.float32)}
    _L1_ffn_in = _L1_ffn_setup()
    _d = {'L0_attn_x': _L0_attn_in['x'], 'L0_attn_w_qkv': _L0_attn_in['w_qkv'], 'L0_attn_w_out': _L0_attn_in['w_out'], 'L0_ffn_w1_w': _L0_ffn_in['w1_w'], 'L0_ffn_w1_s': _L0_ffn_in['w1_s'], 'L0_ffn_w2_w': _L0_ffn_in['w2_w'], 'L0_ffn_w2_s': _L0_ffn_in['w2_s'], 'L0_ffn_h1_w': _L0_ffn_in['h1_w'], 'L0_ffn_h1_s': _L0_ffn_in['h1_s'], 'L0_ffn_h2_w': _L0_ffn_in['h2_w'], 'L0_ffn_h2_s': _L0_ffn_in['h2_s'], 'L0_ffn_w3_w': _L0_ffn_in['w3_w'], 'L0_ffn_w3_s': _L0_ffn_in['w3_s'], 'L1_attn_Wd_q_w': _L1_attn_in['Wd_q_w'], 'L1_attn_Wd_q_b': _L1_attn_in['Wd_q_b'], 'L1_attn_Wu_q_w': _L1_attn_in['Wu_q_w'], 'L1_attn_Wu_q_b': _L1_attn_in['Wu_q_b'], 'L1_attn_Wq_r_w': _L1_attn_in['Wq_r_w'], 'L1_attn_Wq_r_b': _L1_attn_in['Wq_r_b'], 'L1_attn_Wk_r_w': _L1_attn_in['Wk_r_w'], 'L1_attn_Wk_r_b': _L1_attn_in['Wk_r_b'], 'L1_attn_Wd_kv_w': _L1_attn_in['Wd_kv_w'], 'L1_attn_Wd_kv_b': _L1_attn_in['Wd_kv_b'], 'L1_attn_Wu_k_w': _L1_attn_in['Wu_k_w'], 'L1_attn_Wu_k_b': _L1_attn_in['Wu_k_b'], 'L1_attn_Wu_v_w': _L1_attn_in['Wu_v_w'], 'L1_attn_Wu_v_b': _L1_attn_in['Wu_v_b'], 'L1_attn_Wo_w': _L1_attn_in['Wo_w'], 'L1_attn_Wo_b': _L1_attn_in['Wo_b'], 'L1_ffn_gate_w': _L1_ffn_in['gate_w'], 'L1_ffn_gate_b': _L1_ffn_in['gate_b'], 'L1_ffn_w1': _L1_ffn_in['w1'], 'L1_ffn_b1': _L1_ffn_in['b1'], 'L1_ffn_w2': _L1_ffn_in['w2'], 'L1_ffn_b2': _L1_ffn_in['b2']}
    _x0 = _d['L0_attn_x']
    _d['L0_attn_x'] = jax.random.normal(jax.random.fold_in(jax.random.key(seed), 1), (1, 2048, 128), dtype=_x0.dtype)
    del _x0
    return _d

def reference(L0_attn_x, L0_attn_w_qkv, L0_attn_w_out, L0_ffn_w1_w, L0_ffn_w1_s, L0_ffn_w2_w, L0_ffn_w2_s, L0_ffn_h1_w, L0_ffn_h1_s, L0_ffn_h2_w, L0_ffn_h2_s, L0_ffn_w3_w, L0_ffn_w3_s, L1_attn_Wd_q_w, L1_attn_Wd_q_b, L1_attn_Wu_q_w, L1_attn_Wu_q_b, L1_attn_Wq_r_w, L1_attn_Wq_r_b, L1_attn_Wk_r_w, L1_attn_Wk_r_b, L1_attn_Wd_kv_w, L1_attn_Wd_kv_b, L1_attn_Wu_k_w, L1_attn_Wu_k_b, L1_attn_Wu_v_w, L1_attn_Wu_v_b, L1_attn_Wo_w, L1_attn_Wo_b, L1_ffn_gate_w, L1_ffn_gate_b, L1_ffn_w1, L1_ffn_b1, L1_ffn_w2, L1_ffn_b2):

    def _L0_attn_ref(x, w_qkv, w_out):
        import math
        import jax, jax.numpy as jnp
        import numpy as np
        N_HEADS = 16
        THETA = 10000.0

        def _rope_cos_sin(S, head_dim):
            half = head_dim // 2
            inv_freq = 1.0 / THETA ** (jnp.arange(half, dtype=jnp.float32) / half)
            t = jnp.arange(S, dtype=jnp.float32)
            freqs = t[:, None] * inv_freq[None, :]
            return (jnp.cos(freqs), jnp.sin(freqs))

        def _apply_rope(x, cos, sin):
            half = x.shape[-1] // 2
            x1, x2 = (x[..., :half], x[..., half:])
            c = cos[None, None, :, :]
            s = sin[None, None, :, :]
            return jnp.concatenate([x1 * c - x2 * s, x1 * s + x2 * c], axis=-1)
        B, S, D = x.shape
        H = N_HEADS
        hd = D // H
        qkv = x @ w_qkv.T
        q, k, v = jnp.split(qkv, 3, axis=-1)

        def reshape(t):
            return t.reshape(B, S, H, hd).transpose(0, 2, 1, 3)
        q, k, v = (reshape(q), reshape(k), reshape(v))
        cos, sin = _rope_cos_sin(S, hd)
        q = _apply_rope(q.astype(jnp.float32), cos, sin).astype(x.dtype)
        k = _apply_rope(k.astype(jnp.float32), cos, sin).astype(x.dtype)
        scale = math.sqrt(hd)
        scores = jnp.einsum('bhsd,bhtd->bhst', q, k) / scale
        causal = jnp.tril(jnp.ones((S, S), dtype=bool))
        scores = jnp.where(causal[None, None], scores, -jnp.inf)
        attn = jax.nn.softmax(scores.astype(jnp.float32), axis=-1).astype(x.dtype)
        out = jnp.einsum('bhst,bhtd->bhsd', attn, v)
        out = out.transpose(0, 2, 1, 3).reshape(B, S, D)
        return out @ w_out.T

    def _L0_ffn_ref(x, w1_w, w1_s, w2_w, w2_s, h1_w, h1_s, h2_w, h2_s, w3_w, w3_s):
        import jax, jax.numpy as jnp
        import numpy as np
        D_IN, D_HID = (128, 512)

        def _ternary(key, shape):
            return jax.random.randint(key, shape, -1, 2).astype(jnp.float32)

        def _tlin(x, w, s):
            return jnp.einsum('bsi,oi->bso', x, w) * s
        h = jax.nn.silu(_tlin(x, w1_w, w1_s)) * _tlin(x, w2_w, w2_s)
        h = jax.nn.gelu(_tlin(h, h1_w, h1_s), approximate=False)
        h = jax.nn.gelu(_tlin(h, h2_w, h2_s), approximate=False)
        return _tlin(h, w3_w, w3_s)

    def _L1_attn_ref(x, Wd_q_w, Wd_q_b, Wu_q_w, Wu_q_b, Wq_r_w, Wq_r_b, Wk_r_w, Wk_r_b, Wd_kv_w, Wd_kv_b, Wu_k_w, Wu_k_b, Wu_v_w, Wu_v_b, Wo_w, Wo_b):
        import jax, jax.numpy as jnp
        import numpy as np
        NUM_HEAD = 16
        D_Q = 64
        D_KV = 64
        ROPE_BASE = 10000.0

        def _cos_sin(seq_len, dim):
            pos = jnp.arange(seq_len, dtype=jnp.float32)[:, None]
            ids = jnp.arange(dim // 2, dtype=jnp.float32)
            theta = ROPE_BASE ** (-2.0 * ids) / (dim // 2)
            r = pos * theta[None, :]
            return (jnp.cos(r), jnp.sin(r))

        def _rope(x, cos, sin):
            b, s, d = x.shape
            xv = x.reshape(b, s, d // 2, 2)
            x0, x1 = (xv[..., 0], xv[..., 1])
            out = jnp.stack([x0 * cos - x1 * sin, x1 * cos + x0 * sin], axis=-1)
            return out.reshape(b, s, d)
        b, s, d_model = x.shape
        h = NUM_HEAD
        hd = d_model // h
        scale = jnp.sqrt(jnp.float32(h + D_KV + D_Q))

        def heads(t):
            return t.reshape(b, s, h, hd).transpose(0, 2, 1, 3)
        cos, sin = _cos_sin(s, d_model)
        ct_q = x @ Wd_q_w + Wd_q_b
        qt_c = heads(ct_q @ Wu_q_w + Wu_q_b)
        qt_r = heads(_rope(ct_q @ Wq_r_w + Wq_r_b, cos, sin))
        query = qt_c + qt_r
        ct_kv = x @ Wd_kv_w + Wd_kv_b
        kt_c = heads(ct_kv @ Wu_k_w + Wu_k_b)
        kt_r = heads(_rope(x @ Wk_r_w + Wk_r_b, cos, sin))
        key = kt_c + kt_r
        value = heads(ct_kv @ Wu_v_w + Wu_v_b)
        attn = jnp.einsum('bhqd,bhkd->bhqk', query, key) / scale
        attn = jax.nn.softmax(attn, axis=-1)
        out = jnp.einsum('bhqk,bhkd->bhqd', attn, value)
        out = out.transpose(0, 2, 1, 3).reshape(b, s, d_model)
        return out @ Wo_w + Wo_b

    def _L1_ffn_ref(x, gate_w, gate_b, w1, b1, w2, b2):
        import jax, jax.numpy as jnp
        import numpy as np
        NUM_EXPERTS = 8
        TOP_K = 2
        D = 128
        H = 4 * D
        B, S = (4, 256)
        orig_shape = x.shape
        xf = x.reshape(-1, orig_shape[-1])
        gates = xf @ gate_w.T + gate_b
        weights, indices = jax.lax.top_k(gates, TOP_K)
        weights = jax.nn.softmax(weights, axis=-1)
        out = jnp.zeros_like(xf)
        for e in range(NUM_EXPERTS):
            w_e = jnp.sum(weights * (indices == e), axis=-1, keepdims=True)
            h = jax.nn.gelu(xf @ w1[e] + b1[e], approximate=False)
            out = out + w_e * (h @ w2[e] + b2[e])
        return out.reshape(orig_shape)
    x = L0_attn_x
    x = x + _L0_attn_ref(_layernorm(x, axis=-1), L0_attn_w_qkv, L0_attn_w_out)
    x = x + _L0_ffn_ref(_layernorm(x, axis=-1), L0_ffn_w1_w, L0_ffn_w1_s, L0_ffn_w2_w, L0_ffn_w2_s, L0_ffn_h1_w, L0_ffn_h1_s, L0_ffn_h2_w, L0_ffn_h2_s, L0_ffn_w3_w, L0_ffn_w3_s)
    x = x + _L1_attn_ref(_layernorm(x, axis=-1), L1_attn_Wd_q_w, L1_attn_Wd_q_b, L1_attn_Wu_q_w, L1_attn_Wu_q_b, L1_attn_Wq_r_w, L1_attn_Wq_r_b, L1_attn_Wk_r_w, L1_attn_Wk_r_b, L1_attn_Wd_kv_w, L1_attn_Wd_kv_b, L1_attn_Wu_k_w, L1_attn_Wu_k_b, L1_attn_Wu_v_w, L1_attn_Wu_v_b, L1_attn_Wo_w, L1_attn_Wo_b)
    x = x + _L1_ffn_ref(_layernorm(x, axis=-1), L1_ffn_gate_w, L1_ffn_gate_b, L1_ffn_w1, L1_ffn_b1, L1_ffn_w2, L1_ffn_b2)
    return x

_drawn_inputs = setup_inputs


def setup_inputs(seed=0):
    import zlib

    import numpy as np

    out = dict(_drawn_inputs(seed))
    spreads = {'L1_attn_Wd_q_b': (0.0, 0.1),
     'L1_attn_Wu_q_b': (0.0, 0.1),
     'L1_attn_Wq_r_b': (0.0, 0.1),
     'L1_attn_Wk_r_b': (0.0, 0.1),
     'L1_attn_Wd_kv_b': (0.0, 0.1),
     'L1_attn_Wu_k_b': (0.0, 0.1),
     'L1_attn_Wu_v_b': (0.0, 0.1),
     'L1_attn_Wo_b': (0.0, 0.1),
     'L1_ffn_gate_b': (0.0, 0.1),
     'L1_ffn_b1': (0.0, 0.1),
     'L1_ffn_b2': (0.0, 0.1)}
    factors = {}
    for name, (base, spread) in spreads.items():
        noise = np.random.default_rng([zlib.crc32(name.encode()), seed]).standard_normal(out[name].shape)
        drawn = base * np.exp(spread * noise) if base else spread * noise
        out[name] = jnp.asarray(drawn.astype(out[name].dtype))
    for name, factor in factors.items():
        out[name] = (out[name] * factor).astype(out[name].dtype)
    return out
```

```python
from contextlib import ExitStack

import numpy as np

import concourse.bass as bass
from concourse import mybir

F32 = mybir.dt.float32
BF16 = mybir.dt.bfloat16
U32 = mybir.dt.uint32
ALU = mybir.AluOpType
ACT = mybir.ActivationFunctionType
AX = mybir.AxisListType

P = 128
S = 2048
D = 128
H = 16
HD = D // H
T = S // P
CW = 512
C = S // CW
TC = CW // P
HG = 4
G = H // HG
NPART = 3
PROD = NPART * NPART * HD
ROWS = 96
HID = 512
HB = HID // P
E = 8
LAT = 64
EPS = 1e-5
MASKED = -1e30
ONES2 = float(np.array([0x3F803F80], np.uint32).view(np.float32)[0])
SCALE0 = 1.0 / float(np.sqrt(np.float32(HD)))
SCALE1 = 1.0 / float(np.sqrt(np.float32(H + LAT + LAT)))


class Core:
    pass


def norm_phase(nc, k, name, first=False, loads=()):
    with ExitStack() as ctx:
        sem = lambda n: ctx.enter_context(nc.semaphore(f"{name}_{n}"))
        x_loaded, stats_step = [sem(f"x_loaded{c}") for c in range(C if first else 0)], sem("stats_step")
        var_ready, std_ready, xn_ready = sem("var_ready"), sem("std_ready"), sem("xn_ready")
        turned, xnT_ready = sem("turned"), sem("xnT_ready")
        ident_step = sem("ident_step")
        block = ctx.enter_context(nc.Block())

        if first:
            @block.sync
            def _(sp):
                for c in range(C):
                    sp.dma_start(k.x[:, TC * c:TC * (c + 1), :],
                                 k.in_x[TC * P * c:TC * P * (c + 1), :].rearrange("(t p) d -> p t d", p=P)
                                 ).then_inc(x_loaded[c], 16)
                sp.dma_start(k.tables[:, :, :], k.in_tables0.rearrange("a p s -> p a s")).then_inc(k.tables_loaded, 16)
                for dst, src in k.first_loads:
                    sp.dma_start(dst, src).then_inc(k.weights_loaded, 16)

            @block.gpsimd
            def _(pool):
                pool.memset(k.ident[:, :], 0.0).then_inc(ident_step, 1)
                pool.memset(k.mask_qk[:, :], 0.0).then_inc(ident_step, 1)
                pool.memset(k.mask_kq[:, :], 0.0).then_inc(ident_step, 1)
                pool.wait_ge(ident_step, 3)
                pool.affine_select(out=k.ident[:, :], in_=k.ident[:, :], compare_op=ALU.not_equal,
                                   fill=1.0, base=0, pattern=[[-1, P]], channel_multiplier=1
                                   ).then_inc(ident_step, 1)
                pool.affine_select(out=k.mask_qk[:, :], in_=k.mask_qk[:, :], compare_op=ALU.is_ge,
                                   fill=MASKED, base=0, pattern=[[-1, P]], channel_multiplier=1
                                   ).then_inc(ident_step, 1)
                pool.affine_select(out=k.mask_kq[:, :], in_=k.mask_kq[:, :], compare_op=ALU.is_ge,
                                   fill=MASKED, base=0, pattern=[[1, P]], channel_multiplier=-1
                                   ).then_inc(ident_step, 1)
                pool.wait_ge(ident_step, 6)
                pool.tensor_copy(k.ident_bf[:, :], k.ident[:, :]).then_inc(ident_step, 1)
                pool.wait_ge(ident_step, 7)
                pool.memset(k.Qa[64:96, :, :, :].bitcast(F32), 0.0).then_inc(k.zeros_ready, 1)
                ones = k.Ka[64:96, :, :].bitcast(F32)
                for c in range(C):
                    pool.memset(ones[:, :, c * CW // 2:(c + 1) * CW // 2], ONES2).then_inc(k.ones_ready, 1)

        if loads:
            @block.gpsimd
            def _(pool):
                pool.memset(k.Qa[64:96, :, :, :].bitcast(F32), 0.0).then_inc(k.zeros_ready, 1)

            @block.sync
            def _(sp):
                for dst, src in loads:
                    sp.dma_start(dst, src).then_inc(k.weights_loaded, 16)

        @block.vector
        def _(dve):
            for t in range(T):
                if first and t % TC == 0:
                    dve.wait_ge(x_loaded[t // TC], 16)
                last = dve.bn_stats(k.stats[:, t, :], k.x[:, t, :])
            last.then_inc(stats_step, 1)
            dve.wait_ge(stats_step, 1)
            for t in range(T):
                last = dve.bn_aggr(k.mv[:, t, :], k.stats[:, t, :])
            last.then_inc(stats_step, 1)
            dve.wait_ge(stats_step, 2)
            dve.tensor_scalar(k.ve[:, :], k.mv[:, :, 1], EPS, None, ALU.add).then_inc(var_ready, 1)
            dve.wait_ge(std_ready, 1)
            dve.reciprocal(k.rstd[:, :], k.std[:, :]).then_inc(stats_step, 1)
            dve.wait_ge(stats_step, 3)
            for t in range(T):
                dve.tensor_scalar(k.xn[:, t, :], k.x[:, t, :], k.mv[:, t, 0:1], k.rstd[:, t:t + 1],
                                  ALU.subtract, ALU.mult).then_inc(xn_ready, 1)

        @block.scalar
        def _(act):
            act.wait_ge(var_ready, 1)
            act.activation(k.std[:, :], k.ve[:, :], ACT.Sqrt).then_inc(std_ready, 1)
            for c in range(C):
                act.wait_ge(turned, c + 1)
                act.activation(k.xnT[:, c * CW:(c + 1) * CW], k.bank[c][:, :], ACT.Copy
                               ).then_inc(xnT_ready, 1)

        @block.tensor
        def _(pe):
            if first:
                pe.wait_ge(ident_step, 7)
            for t in range(T):
                pe.wait_ge(xn_ready, t + 1)
                mm = pe.transpose(k.bank[t // TC][:, t % TC * P:(t % TC + 1) * P], k.xn[:, t, :], k.ident[:, :])
                if t % TC == TC - 1:
                    mm.then_inc(turned, 1)


def project_phase(nc, k, layer):
    n = f"proj{layer}"
    items = [(c, w) for c in range(C) for w in (0, 1)]
    with ExitStack() as ctx:
        sem = lambda s: ctx.enter_context(nc.semaphore(f"{n}_{s}"))
        lat_psum, lat_ready = sem("lat_psum"), sem("lat_ready")
        qk_psum, rotated, v_psum, v_copied = sem("qk_psum"), sem("rotated"), sem("v_psum"), sem("v_copied")
        u_added = sem("u_added")
        summed, part1, rest1, part2, part3 = sem("summed"), sem("part1"), sem("rest1"), sem("part2"), sem("part3")
        parts_stored, ones_row = [sem("q_parts_stored"), sem("k_parts_stored")], sem("ones_row")
        block = ctx.enter_context(nc.Block())
        A, B, U = k.bank[0:2], k.bank[2:4], k.bank[4:6]
        LATP, VP = k.bank[6], k.bank[7]
        table_c, table_s = k.tables[:, 0, :], k.tables[:, 1, :]

        @block.sync
        def _(sp):
            if layer == 1:
                sp.dma_start(k.tables[:, :, :], k.in_tables1.rearrange("a p s -> p a s")).then_inc(k.tables_loaded, 16)

            def lay_out(c):
                for stored in parts_stored:
                    sp.wait_ge(stored, 16 * (c + 1))
                sp.wait_ge(k.zeros_ready, layer + 1)
                if layer == 0:
                    sp.wait_ge(k.ones_ready, c + 1)
                for a in range(NPART):
                    rows = slice(a * NPART * HD, (a + 1) * NPART * HD)
                    for b in range(NPART):
                        r = slice(rows.start + b * HD, rows.start + (b + 1) * HD)
                        src = k.parts[0][a, :, c * CW:(c + 1) * CW].rearrange("(h d) s -> d h s", d=HD)
                        sp.dma_start(k.Qa[r, c * G:(c + 1) * G, :, :].rearrange("d g j s -> d (g j) s"), src
                                     ).then_inc(k.laid_out[layer], 16)
                        src = k.parts[1][b, :, c * CW:(c + 1) * CW].rearrange("(h d) s -> d h s", d=HD)
                        sp.dma_start(k.Ka[r, :, c * CW:(c + 1) * CW], src).then_inc(k.laid_out[layer], 16)

            for i, (c, w) in enumerate(items):
                sp.wait_ge(part3, i + 1)
                sp.dma_start(k.parts[w][:, :, c * CW:(c + 1) * CW].rearrange("a p s -> p a s"),
                             k.part_buf[:, i % 2, :, :]).then_inc(parts_stored[w], 16)
                if w == 1:
                    lay_out(c)

        @block.tensor
        def _(pe):
            pe.wait_ge(k.weights_loaded, 16 * (len(k.first_loads) + layer * len(k.latent_loads)))
            if layer == 1:
                pe.wait_ge(ones_row, 1)
            for c in range(C):
                xc = k.xnT[:, c * CW:(c + 1) * CW]
                if layer == 1:
                    if c >= 1:
                        pe.wait_ge(lat_ready, 2 * c)
                    pe.matmul(LATP[:, :], k.w_down[:, :], xc, start=True, stop=True).then_inc(lat_psum, 1)
                    pe.wait_ge(lat_ready, 2 * (c + 1))
                for w in (0, 1):
                    i = 2 * c + w
                    if i >= 2:
                        pe.wait_ge(rotated, i - 1)
                    if layer == 0:
                        pe.matmul(A[w][:, :], k.w_qk[:, w, 0, :], xc, start=True, stop=True)
                        mm = pe.matmul(B[w][:, :], k.w_qk[:, w, 1, :], xc, start=True, stop=True)
                    elif w == 0:
                        lq = k.latent[:, c % 2, 0, :]
                        pe.matmul(A[w][:, :], k.w_qr[:, 0, :], lq, start=True, stop=True)
                        pe.matmul(B[w][:, :], k.w_qr[:, 1, :], lq, start=True, stop=True)
                        mm = pe.matmul(U[w][:, :], k.w_up[:, 0, :], lq, start=True, stop=True)
                    else:
                        lk = k.latent[:, c % 2, 1, :]
                        pe.matmul(A[w][:, :], k.w_kr[:, 0, :], xc, start=True, stop=True)
                        pe.matmul(B[w][:, :], k.w_kr[:, 1, :], xc, start=True, stop=True)
                        mm = pe.matmul(U[w][:, :], k.w_up[:, 1, :], lk, start=True, stop=True)
                    mm.then_inc(qk_psum, 1)
                if c >= 1:
                    pe.wait_ge(v_copied, c)
                for t in range(TC):
                    if layer == 0:
                        mm = pe.matmul(VP[:, t * P:(t + 1) * P], xc[:, t * P:(t + 1) * P], k.w_v[:, :],
                                       start=True, stop=True)
                    else:
                        mm = pe.matmul(VP[:, t * P:(t + 1) * P], k.latent[:, c % 2, 1, t * P:(t + 1) * P],
                                       k.w_up[:, 2, :], start=True, stop=True)
                mm.then_inc(v_psum, 1)

        @block.vector
        def _(dve):
            if layer == 1:
                dve.memset(k.latent[LAT:LAT + 1, :, :, :], 1.0).then_inc(ones_row, 1)
            dve.wait_ge(k.tables_loaded, 16 * (layer + 1))

            def rotate(i):
                c, w = items[i]
                dve.wait_ge(qk_psum, i + 1)
                if i >= 2:
                    dve.wait_ge(summed, i - 1)
                    dve.wait_ge(part3, i - 1)
                tc_, ts_ = table_c[:, c * CW:(c + 1) * CW], table_s[:, c * CW:(c + 1) * CW]
                t1, t2 = k.t1[:, w, :], k.t2[:, w, :]
                if layer == 0:
                    dve.tensor_tensor(t1, A[w][:, :], tc_, ALU.mult)
                    dve.tensor_tensor(t2, B[w][:, :], ts_, ALU.mult).then_inc(rotated, 1)
                    return
                if w == 0:
                    dve.tensor_tensor(t2, B[w][:, :], ts_, ALU.mult)
                    dve.tensor_tensor(t1, A[w][:, :], tc_, ALU.mult).then_inc(u_added, 1)
                else:
                    dve.scalar_tensor_tensor(t2, B[w][:, :], k.b_kr[:, 1:2], ts_, ALU.add, ALU.mult)
                    dve.scalar_tensor_tensor(t1, A[w][:, :], k.b_kr[:, 0:1], tc_, ALU.add, ALU.mult
                                             ).then_inc(u_added, 1)
                dve.wait_ge(u_added, i + 1)
                dve.tensor_tensor(t1, U[w][:, :], t1, ALU.add).then_inc(rotated, 1)

            def first_rest(i):
                w = items[i][1]
                dve.wait_ge(part1, i + 1)
                dve.tensor_tensor(k.rest[:, w, :], k.full[:, w, :], k.part_buf[:, w, 0, :], ALU.subtract
                                  ).then_inc(rest1, 1)

            def second_rest(i):
                w = items[i][1]
                dve.wait_ge(part2, i + 1)
                dve.tensor_tensor(k.part_buf[:, w, 2, :], k.rest[:, w, :], k.part_buf[:, w, 1, :], ALU.subtract
                                  ).then_inc(part3, 1)

            for i in range(len(items) + 2):
                if i >= 2:
                    second_rest(i - 2)
                if i < len(items):
                    rotate(i)
                if 1 <= i <= len(items):
                    first_rest(i - 1)

        @block.gpsimd
        def _(pool):
            for i, (c, w) in enumerate(items):
                pool.wait_ge(rotated, i + 1)
                if i >= 2:
                    pool.wait_ge(rest1, i - 1)
                pool.tensor_tensor(k.full[:, w, :], k.t1[:, w, :], k.t2[:, w, :], ALU.add).then_inc(summed, 1)

        @block.scalar
        def _(act):
            def latents(c):
                act.wait_ge(lat_psum, c + 1)
                if c >= 2:
                    act.wait_ge(v_psum, c - 1)
                for a in (0, 1):
                    act.activation(k.latent[0:LAT, c % 2, a, :], LATP[LAT * a:LAT * (a + 1), :], ACT.Identity,
                                   bias=k.b_down[LAT * a:LAT * (a + 1), :]).then_inc(lat_ready, 1)

            def first_part(i):
                w = items[i][1]
                act.wait_ge(summed, i + 1)
                if i >= 2:
                    act.wait_ge(parts_stored[w], 16 * (i // 2))
                act.activation(k.part_buf[:, w, 0, :], k.full[:, w, :], ACT.Copy).then_inc(part1, 1)

            def second_part(i):
                w = items[i][1]
                act.wait_ge(rest1, i + 1)
                act.activation(k.part_buf[:, w, 1, :], k.rest[:, w, :], ACT.Copy).then_inc(part2, 1)

            def values(c):
                act.wait_ge(v_psum, c + 1)
                act.activation(k.V[:, TC * c:TC * (c + 1), :], VP[:, :].rearrange("p (t d) -> p t d", t=TC), ACT.Copy
                               ).then_inc(v_copied, 1)

            if layer == 1:
                act.wait_ge(k.weights_loaded, 16 * len(k.first_loads))
                latents(0)
            for i, (c, w) in enumerate(items):
                first_part(i)
                if i >= 1:
                    second_part(i - 1)
                if w == 0:
                    values(c)
                    if layer == 1 and c + 1 < C:
                        latents(c + 1)
            second_part(len(items) - 1)


def attention_phase(nc, k, layer):
    causal = layer == 0
    scale = SCALE0 if causal else SCALE1
    steps = lambda c: TC * (c + 1) if causal else T
    def pieces(c):
        out = []
        for t in range(TC):
            keys = (TC * c + t + 1) * P if causal else S
            for j in range(HG):
                out += [(t, j, a, min(CW, keys - a)) for a in range(0, keys, CW)]
        return out

    ahead = lambda c: len(pieces(c)) * (6 if causal else 3) // 8

    def step0(c, g):
        if not causal:
            return (c * G + g) * T
        return sum(G * steps(i) for i in range(c)) + g * steps(c)

    def piece0(c, g):
        if not causal:
            return (c * G + g) * len(pieces(0))
        return sum(G * len(pieces(i)) for i in range(c)) + g * len(pieces(c))

    FREE = 4

    def max_bank(c, i):
        return 1 if len(pieces(c)) % 3 == 1 and i == len(pieces(c)) - 1 else i % 3

    def pieces_back(c, before, i):
        row = [max_bank(before, n) for n in range(len(pieces(before)))] + [max_bank(c, n) for n in range(i)]
        return row[::-1].index(max_bank(c, i)) + 1
    name = f"attn{layer}"
    with ExitStack() as ctx:
        sem = lambda s: ctx.enter_context(nc.semaphore(f"{name}_{s}"))
        scores_ready, probs_ready, pv_done, acc_free = sem("scores_ready"), sem("probs_ready"), sem("pv_done"), sem("acc_free")
        max_scores, max_read, v_staged = sem("max_scores"), sem("max_read"), sem("v_staged")
        shift_step, shift_ready, shift_stored, shift_rows = sem("shift_step"), sem("shift_ready"), sem("shift_stored"), sem("shift_rows")
        staged_zero = sem("staged_zero")
        block = ctx.enter_context(nc.Block())
        acc = k.bank[7]
        score, for_max = k.bank[0:4], k.bank[4:7]

        def schedule(unit):
            def units_of(eng, c, more):
                with eng.Fori(0, G - 2) as g:
                    unit(c, g, (c, g + 1), (c, g + 2))
                unit(c, G - 2, (c, G - 1), (c + 1, 0) if more else None)
                unit(c, G - 1, *(((c + 1, 0), (c + 1, 1)) if more else (None, None)))

            def run(eng):
                if causal:
                    for c in range(C):
                        units_of(eng, c, c + 1 < C)
                else:
                    with eng.Fori(0, C - 1) as c:
                        units_of(eng, c, True)
                    units_of(eng, C - 1, False)
            return run

        shape_c = lambda c: c if causal else 0

        def last_pieces(unit):
            return [(*unit, i) for i in range(ahead(shape_c(unit[0])), len(pieces(shape_c(unit[0]))))] if unit else []

        def first_pieces(unit):
            return [(*unit, i) for i in range(ahead(shape_c(unit[0])))] if unit else []

        @block.tensor
        def _(pe):
            def max_piece(c, g, i):
                t, j, a, w = pieces(shape_c(c))[i]
                n = c * G + g
                before = max(c - 1, 0) if causal and isinstance(g, int) and g == 0 else shape_c(c)
                pe.wait_ge(max_read, FREE + piece0(c, g) + i - pieces_back(shape_c(c), before, i) + 1)
                bank = for_max[max_bank(shape_c(c), i)]
                diagonal = causal and a + w == (TC * c + t + 1) * P
                mm = pe.matmul(bank[:, 0:w], k.Qa[0:ROWS, n, j, t * P:(t + 1) * P],
                               k.Ka[0:ROWS, g * HG + j, a:a + w], start=True, stop=not diagonal)
                if diagonal:
                    mm = pe.matmul(bank[:, w - P:w], k.ident_bf[:, :], k.mask_qk[:, :], start=False, stop=True)
                mm.then_inc(max_scores, 1)

            def scores(c, g, kt, j):
                e = 4 * (step0(c, g) + kt) + j
                n = c * G + g
                first = max(0, kt - TC * c) * P if causal else 0
                diagonal = causal and kt >= TC * c
                pe.wait_ge(probs_ready, FREE + e - 4 + 1)
                bank = score[j]
                mm = pe.matmul(bank[:, first:CW], k.Ka[0:ROWS, g * HG + j, kt * P:(kt + 1) * P],
                               k.Qa[0:ROWS, n, j, first:CW], start=True, stop=not diagonal)
                if diagonal:
                    mm = pe.matmul(bank[:, first:first + P], k.ident_bf[:, :], k.mask_kq[:, :],
                                   start=False, stop=True)
                mm.then_inc(scores_ready, 1)

            def values(c, g, kt):
                s = step0(c, g) + kt
                first = max(0, kt - TC * c) * P if causal else 0
                pe.wait_ge(probs_ready, FREE + 4 * s + 4)
                pe.wait_ge(v_staged, s + 1)
                if kt == 0:
                    pe.wait_ge(acc_free, c * G + g + 1)
                slot = 4 * (kt % 2)
                for j in range(HG):
                    mm = pe.matmul(acc[32 * j:32 * j + 32, first:CW], k.Vst[:, kt, j, :],
                                   k.probs[:, slot + j, first:CW], start=(kt == 0),
                                   stop=(kt == steps(shape_c(c)) - 1))
                mm.then_inc(pv_done, 1)

            def unit(c, g, following, second):
                n_steps = steps(shape_c(c))
                todo = last_pieces(following) + first_pieces(second)
                width = [CW - (max(0, kt - TC * c) * P if causal else 0) for kt in range(n_steps) for _ in range(HG)]
                cost = [pieces(shape_c(p[0]))[p[2]][3] + P for p in todo]
                done = [0]
                pe.wait_ge(shift_rows, 128 * (c * G + g) + 256)

                def some_maxima(slot):
                    while done[0] < len(todo) and (slot == len(width) - 1 or sum(cost[:done[0]]) * sum(width)
                                                   < sum(width[:slot + 1]) * sum(cost)):
                        max_piece(*todo[done[0]])
                        done[0] += 1

                for kt in range(n_steps):
                    for j in range(HG):
                        scores(c, g, kt, j)
                        some_maxima(HG * kt + j)
                    if kt:
                        values(c, g, kt - 1)
                values(c, g, n_steps - 1)

            pe.wait_ge(k.laid_out[layer], 16 * 18 * C)
            for piece in first_pieces((0, 0)) + last_pieces((0, 0)) + first_pieces((0, 1)):
                max_piece(*piece)
            schedule(unit)(pe)

        @block.scalar
        def _(act):
            act.sem_inc(probs_ready, FREE)
            def unit(c, g, *_):
                for kt in range(steps(shape_c(c))):
                    s = step0(c, g) + kt
                    first = max(0, kt - TC * c) * P if causal else 0
                    act.wait_ge(pv_done, s + 1)
                    for j in range(HG):
                        act.wait_ge(scores_ready, 4 * s + j + 1)
                        act.activation(k.probs[:, 4 * (kt % 2) + j, first:CW], score[j][:, first:CW],
                                       ACT.Exp, scale=scale).then_inc(probs_ready, 1)
            schedule(unit)(act)

        @block.vector
        def _(dve):
            dve.sem_inc(max_read, FREE)
            dve.sem_inc(acc_free, 1)
            dve.memset(k.negsplit[:, :, :], 0.0).then_inc(shift_step, 1)

            def reduce(c, g, i):
                t, j, a, w = pieces(shape_c(c))[i]
                dve.wait_ge(max_scores, piece0(c, g) + i + 1)
                if i == 0:
                    dve.wait_ge(shift_step, 1 + 4 * (c * G + g) - 3 if not isinstance(c * G + g, int) or c * G + g else 1)
                dve.tensor_reduce(k.maxp[:, a // CW, t, j:j + 1], for_max[max_bank(shape_c(c), i)][:, 0:w], AX.X, ALU.max
                                  ).then_inc(max_read, 1)

            def shift_steps(c, g):
                n = c * G + g
                n_keys = shape_c(c) + 1 if causal else C
                after = lambda i: 1 + 4 * n + i

                def maximum():
                    dve.wait_ge(max_read, FREE + piece0(c, g) + len(pieces(shape_c(c))))
                    if n_keys == 1:
                        dve.tensor_copy(k.maxu[:, :, :], k.maxp[:, 0, :, :]).then_inc(shift_step, 1)
                    else:
                        dve.tensor_reduce(k.maxu[:, :, :].rearrange("p t j -> p (t j)"),
                                          k.maxp[:, 0:n_keys, :, :].rearrange("p i t j -> p (t j) i"), AX.X, ALU.max
                                          ).then_inc(shift_step, 1)

                def first_part():
                    dve.wait_ge(shift_step, after(1))
                    dve.tensor_scalar(k.negsplit[:, :, 0:HG], k.maxu[:, :, :], -1.0, None, ALU.mult
                                      ).then_inc(shift_step, 1)

                def second_part():
                    dve.wait_ge(shift_step, after(2))
                    dve.scalar_tensor_tensor(k.negsplit[:, :, HG:2 * HG], k.maxu[:, :, :], -1.0,
                                             k.negsplit[:, :, 0:HG], ALU.mult, ALU.subtract).then_inc(shift_step, 1)

                def turn():
                    dve.wait_ge(shift_step, after(3))
                    dve.wait_ge(shift_stored, 16 * n + 16)
                    dve.transpose(k.shiftT[:, :], k.negsplit[:, :, :].rearrange("p t c -> p (t c)")
                                  ).then_inc(shift_step, 1)

                return [maximum, first_part, second_part, turn]

            def maxima(following, second):
                for piece in last_pieces(following):
                    reduce(*piece)
                todo = shift_steps(*following) if following else []
                if todo:
                    todo.pop(0)()
                for piece in first_pieces(second):
                    reduce(*piece)
                    if todo:
                        todo.pop(0)()
                for step in todo:
                    step()

            def unit(c, g, following, second):
                maxima(following, second)
                dve.wait_ge(pv_done, 2 + step0(c, g) + steps(shape_c(c)))
                dve.tensor_copy(k.outT(c * G + g), acc[:, :]).then_inc(acc_free, 1)

            for piece in first_pieces((0, 0)):
                reduce(*piece)
            maxima((0, 0), (0, 1))
            schedule(unit)(dve)

        @block.sync
        def _(sp):
            sp.sem_inc(shift_stored, 16)
            sp.sem_inc(shift_rows, 128)
            for dst, src in k.attention_loads[layer]:
                sp.dma_start(dst, src).then_inc(k.next_loaded[layer], 16)

            def unit(n):
                sp.wait_ge(shift_step, 1 + 4 * n + 4)
                sp.wait_ge(shift_rows, 128 * n + 128)
                sp.dma_start(k.shift_dram[:, :], k.shiftT[:, :]).then_inc(shift_stored, 16)
                sp.wait_ge(shift_stored, 16 * n + 32)
                for r in range(2):
                    src = k.shift_dram.rearrange("(b c) (t q) -> c t b q", b=4, t=TC)[r * HG:(r + 1) * HG]
                    for j in range(HG):
                        sp.dma_start(k.Qa[PROD + r:PROD + r + 1, n, j, :].rearrange("o (t b q) -> o t b q", t=TC, b=4),
                                     src[j:j + 1]).then_inc(shift_rows, 16)
            with sp.Fori(0, C * G) as n:
                unit(n)

        @block.gpsimd
        def _(pool):
            pool.sem_inc(pv_done, 2)
            pool.memset(k.Vst[:, :, :, :], 0.0).then_inc(staged_zero, 1)
            pool.wait_ge(staged_zero, 1)
            pool.memset(k.Vst[:, :, :, HD:HD + 1], 1.0).then_inc(staged_zero, 1)
            pool.wait_ge(staged_zero, 2)

            def stage(c, g, kt, wait):
                if wait is not None:
                    pool.wait_ge(pv_done, 2 + wait + 1)
                pool.tensor_copy(k.Vst[:, kt, :, 0:HD],
                                 k.V[:, kt, bass.ds(g * HG * HD, HG * HD)].rearrange("p (j d) -> p j d", j=HG)
                                 ).then_inc(v_staged, 1)

            def units(c, first, last):
                with pool.Fori(first, last) as g:
                    for kt in range(steps(shape_c(c))):
                        stage(c, g, kt, step0(c, g) - steps(shape_c(c)) + kt)

            if causal:
                for c in range(C):
                    before = steps(c - 1) if c else 0
                    for kt in range(steps(c)):
                        stage(c, 0, kt, step0(c, 0) - before + kt if kt < before else None)
                    units(c, 1, G)
            else:
                for kt in range(T):
                    stage(0, 0, kt, None)
                units(0, 1, G)
                with pool.Fori(1, C) as c:
                    with pool.Fori(0, G) as g:
                        for kt in range(T):
                            stage(c, g, kt, step0(c, g) - T + kt)


def output_phase(nc, k, layer):
    name = f"out{layer}"
    with ExitStack() as ctx:
        sem = lambda s: ctx.enter_context(nc.semaphore(f"{name}_{s}"))
        turned, inverse, heads_ready, heads_turned, headsT_ready = (
            sem("turned"), sem("inverse"), sem("heads_ready"), sem("heads_turned"), sem("headsT_ready"))
        projected, added, bias_added = sem("projected"), sem("added"), sem("bias_added")
        block = ctx.enter_context(nc.Block())
        tb, hb, yb = k.bank[0:2], k.bank[2:4], k.bank[4:6]
        w_out = k.w_out[layer]

        @block.tensor
        def _(pe):
            def turn(i):
                c, t = divmod(i, TC)
                if i >= 2:
                    pe.wait_ge(heads_ready, i - 1)
                for g in range(G):
                    mm = pe.transpose(tb[i % 2][:, g * P:(g + 1) * P],
                                      k.outT(c * G + g)[:, t * P:(t + 1) * P], k.ident[:, :])
                mm.then_inc(turned, 1)

            def turn_heads(i):
                pe.wait_ge(heads_ready, i + 1)
                if i >= 2:
                    pe.wait_ge(headsT_ready, i - 1)
                pe.transpose(hb[i % 2][:, 0:P], k.heads[:, i % 2, :], k.ident[:, :]).then_inc(heads_turned, 1)

            def project(i):
                pe.wait_ge(headsT_ready, i + 1)
                if i >= 2:
                    pe.wait_ge(added, i - 1)
                pe.matmul(yb[i % 2][:, 0:D], k.headsT[:, i % 2, :], w_out[:, :], start=True, stop=True
                          ).then_inc(projected, 1)

            for i in range(T + 2):
                if i < T:
                    turn(i)
                if 1 <= i <= T:
                    turn_heads(i - 1)
                if i >= 2:
                    project(i - 2)

        @block.vector
        def _(dve):
            def normalise(i):
                src = tb[i % 2][:, :].rearrange("p (h w) -> p h w", w=32)
                dve.wait_ge(turned, i + 1)
                if i >= 2:
                    dve.wait_ge(heads_ready, i - 1)
                dve.reciprocal(k.inv[:, i % 2, :], src[:, :, HD]).then_inc(inverse, 1)
                dve.wait_ge(inverse, i + 1)
                if i >= 2:
                    dve.wait_ge(heads_turned, i - 1)
                dve.tensor_tensor(k.heads[:, i % 2, :].rearrange("p (h d) -> p h d", d=HD), src[:, :, 0:HD],
                                  k.inv[:, i % 2, :].unsqueeze(2).to_broadcast([P, H, HD]), ALU.mult
                                  ).then_inc(heads_ready, 1)

            def add(i):
                dve.wait_ge(projected, i + 1)
                if layer == 1:
                    dve.tensor_tensor(k.x[:, i, :], k.x[:, i, :], k.bo_rows[:, :], ALU.add).then_inc(bias_added, 1)
                    dve.wait_ge(bias_added, i + 1)
                dve.tensor_tensor(k.x[:, i, :], yb[i % 2][:, 0:D], k.x[:, i, :], ALU.add).then_inc(added, 1)

            for i in range(T + 2):
                if i < T:
                    normalise(i)
                if i >= 2:
                    add(i - 2)

        @block.scalar
        def _(act):
            for i in range(T):
                act.wait_ge(heads_turned, i + 1)
                if i >= 2:
                    act.wait_ge(projected, i - 1)
                act.activation(k.headsT[:, i % 2, :], hb[i % 2][:, 0:P], ACT.Copy).then_inc(headsT_ready, 1)


def ffn_phase(nc, k):
    with ExitStack() as ctx:
        sem = lambda s: ctx.enter_context(nc.semaphore(f"ffn_{s}"))
        up_ready, silu_ready, gated = sem("up_ready"), sem("silu_ready"), sem("gated")
        h_ready, h_done, y_ready, y_scaled, y_added = sem("h_ready"), sem("h_done"), sem("y_ready"), sem("y_scaled"), sem("y_added")
        block = ctx.enter_context(nc.Block())
        up1, up2, hb, yb = k.bank[0:2], k.bank[2:4], k.bank[4:6], k.bank[6]

        @block.tensor
        def _(pe):
            pe.wait_ge(k.next_loaded[0], 16 * len(k.attention_loads[0]))
            with pe.Fori(0, C) as c:
                xc = k.xnT[:, bass.ds(c * CW, CW)]
                for m in range(HB):
                    pe.wait_ge(gated, 4 * c + m + 1)
                    pe.matmul(up1[m % 2][:, :], k.w1[:, m * P:(m + 1) * P], xc, start=True, stop=True)
                    pe.matmul(up2[m % 2][:, :], k.w2[:, m * P:(m + 1) * P], xc, start=True, stop=True
                              ).then_inc(up_ready, 1)
                for layer, (w, src) in enumerate(((k.h1, k.act_g), (k.h2, k.act_1))):
                    for m in range(HB):
                        pe.wait_ge(h_done, 8 * c + 4 * layer + m + 1)
                        for b in range(HB):
                            if m == 0:
                                if layer == 0:
                                    pe.wait_ge(gated, 2 + 4 * c + b + 1)
                                else:
                                    pe.wait_ge(h_done, 2 + 8 * c + b + 1)
                            mm = pe.matmul(hb[m % 2][:, :], w[:, b, m * P:(m + 1) * P], src[:, b, :],
                                           start=(b == 0), stop=(b == HB - 1))
                        mm.then_inc(h_ready, 1)
                pe.wait_ge(h_done, 2 + 8 * c + 8)
                pe.wait_ge(y_added, 4 * c + 1)
                for t in range(TC):
                    for b in range(HB):
                        mm = pe.matmul(yb[:, t * P:(t + 1) * P], k.act_2[:, b, t * P:(t + 1) * P], k.w3[:, b, :],
                                       start=(b == 0), stop=(b == HB - 1))
                mm.then_inc(y_ready, 1)

        @block.scalar
        def _(act):
            act.sem_inc(h_done, 2)
            with act.Fori(0, C) as c:
                for m in range(HB):
                    act.wait_ge(up_ready, 4 * c + m + 1)
                    act.wait_ge(gated, 4 * c + m + 1)
                    act.activation(k.silu[:, m % 2, :], up1[m % 2][:, :], ACT.Silu, scale=k.s1[:, m:m + 1]
                                   ).then_inc(silu_ready, 1)
                for layer, (s, dst) in enumerate(((k.sh1, k.act_1), (k.sh2, k.act_2))):
                    for m in range(HB):
                        act.wait_ge(h_ready, 8 * c + 4 * layer + m + 1)
                        act.activation(dst[:, m, :], hb[m % 2][:, :], ACT.Gelu, scale=s[:, m:m + 1]
                                       ).then_inc(h_done, 1)

        @block.vector
        def _(dve):
            dve.sem_inc(gated, 2)
            dve.sem_inc(y_added, 1)
            with dve.Fori(0, C) as c:
                for m in range(HB):
                    dve.wait_ge(silu_ready, 4 * c + m + 1)
                    dve.scalar_tensor_tensor(k.act_g[:, m, :], up2[m % 2][:, :], k.s2[:, m:m + 1],
                                             k.silu[:, m % 2, :], ALU.mult, ALU.mult).then_inc(gated, 1)
                dve.wait_ge(y_ready, c + 1)
                dve.wait_ge(y_added, 4 * c + 1)
                for t in range(TC):
                    dve.tensor_tensor(k.y_tmp[:, t, :], yb[:, t * P:(t + 1) * P], k.s3_rows[:, :], ALU.mult
                                      ).then_inc(y_scaled, 1)
                for t in range(TC):
                    dve.wait_ge(y_scaled, 4 * c + t + 1)
                    xt = k.x[:, bass.ds(c * TC + t, 1), :]
                    dve.tensor_tensor(xt, xt, k.y_tmp[:, t:t + 1, :], ALU.add).then_inc(y_added, 1)


def gate_phase(nc, k):
    with ExitStack() as ctx:
        sem = lambda s: ctx.enter_context(nc.semaphore(f"gate_{s}"))
        gates, step, weights_ready, expd, turned, weightsT, bias_ready, iota_ready = (
            sem("gates"), sem("step"), sem("weights_ready"), sem("expd"), sem("turned"), sem("weightsT"), sem("bias_ready"), sem("iota"))
        block = ctx.enter_context(nc.Block())

        @block.tensor
        def _(pe):
            pe.wait_ge(k.next_loaded[1], 16 * len(k.attention_loads[1]))
            for t in range(T):
                mm = pe.matmul(k.bank[0][:, t * E:(t + 1) * E], k.xnT[:, t * P:(t + 1) * P], k.gate_w[:, :],
                               start=True, stop=True)
            mm.then_inc(gates, 1)
            pe.wait_ge(weights_ready, 1)
            for t in range(T):
                mm = pe.transpose(k.bank[1 + t // TC][0:E, t % TC * P:(t % TC + 1) * P], k.wts[:, t, :], k.ident[:, :])
            mm.then_inc(turned, 1)
            for t in range(T):
                if t % TC == 0:
                    pe.wait_ge(weightsT, t // TC + 1)
                    if t:
                        pe.wait_ge(bias_ready, t - TC + 4)
                mm = pe.matmul(k.bank[5][:, t % TC * P:(t % TC + 1) * P], k.wtsT[:, t * P:(t + 1) * P], k.b2[:, :],
                               start=True, stop=True)
                if t % TC == TC - 1:
                    mm.then_inc(turned, 1)

        @block.gpsimd
        def _(pool):
            pool.iota(k.expert_i[:, :], pattern=[[1, E]], base=0, channel_multiplier=0).then_inc(iota_ready, 1)
            pool.wait_ge(iota_ready, 1)
            pool.tensor_copy(k.expert[:, :], k.expert_i[:, :]).then_inc(iota_ready, 1)

        @block.scalar
        def _(act):
            act.wait_ge(expd, 1)
            act.activation(k.g_exp[:, :], k.g_diff[:, :], ACT.Exp).then_inc(expd, 1)
            for c in range(C):
                act.wait_ge(turned, 1)
                act.activation(k.wtsT[:, c * CW:(c + 1) * CW], k.bank[1 + c][0:E, :], ACT.Copy).then_inc(weightsT, 1)

        @block.vector
        def _(dve):
            n = [0]

            def done(ins):
                n[0] += 1
                ins.then_inc(step, 1)
                dve.wait_ge(step, n[0])

            dve.wait_ge(k.next_loaded[1], 16 * len(k.attention_loads[1]))
            dve.wait_ge(gates, 1)
            g_psum = k.bank[0][:, 0:T * E].rearrange("p (t e) -> p t e", e=E)
            done(dve.tensor_tensor(k.g[:, :, :], g_psum, k.gate_b_rows[:, :].unsqueeze(1).to_broadcast([P, T, E]), ALU.add))
            for t in range(T):
                last = dve.max(k.top[:, t, :], k.g[:, t, :])
            done(last)
            for t in range(T):
                last = dve.max_index(k.top_i[:, t, :], k.top[:, t, :], k.g[:, t, :])
            done(last)
            dve.tensor_copy(k.top_f[:, :, :], k.top_i[:, :, 0:2])
            dve.tensor_tensor(k.g_diff[:, :], k.top[:, :, 1], k.top[:, :, 0], ALU.subtract).then_inc(expd, 1)
            dve.wait_ge(expd, 2)
            done(dve.tensor_scalar(k.g_sum[:, :], k.g_exp[:, :], 1.0, None, ALU.add))
            done(dve.reciprocal(k.p1[:, :], k.g_sum[:, :]))
            done(dve.tensor_tensor(k.p2[:, :], k.g_exp[:, :], k.p1[:, :], ALU.mult))
            dve.wait_ge(iota_ready, 2)
            for r, p in ((0, k.p1), (1, k.p2)):
                hit = k.hit[:, r, :, :]
                done(dve.tensor_tensor(hit, k.expert[:, :].unsqueeze(1).to_broadcast([P, T, E]),
                                       k.top_f[:, :, r:r + 1].to_broadcast([P, T, E]), ALU.is_equal))
                done(dve.tensor_tensor(hit, hit, p[:, :].unsqueeze(2).to_broadcast([P, T, E]), ALU.mult))
            dve.tensor_tensor(k.wts[:, :, :], k.hit[:, 0, :, :], k.hit[:, 1, :, :], ALU.add).then_inc(weights_ready, 1)
            for t in range(T):
                if t % TC == 0:
                    dve.wait_ge(turned, 2 + t // TC)
                dve.tensor_tensor(k.x[:, t, :], k.bank[5][:, t % TC * P:(t % TC + 1) * P], k.x[:, t, :], ALU.add
                                  ).then_inc(bias_ready, 1)


def experts_phase(nc, k):
    with ExitStack() as ctx:
        sem = lambda s: ctx.enter_context(nc.semaphore(f"moe_{s}"))
        w_loaded = [sem("w_loaded0"), sem("w_loaded1")]
        up_ready, act_ready, y_ready, y_added, stored = sem("up_ready"), sem("act_ready"), sem("y_ready"), sem("y_added"), sem("stored")
        block = ctx.enter_context(nc.Block())
        ub, yb = k.bank[0:4], k.bank[4:6]

        @block.sync
        def _(sp):
            def load(e, q):
                sp.dma_start(k.ew1[:, q, :], k.in_ew1[bass.ds(e, 1)].rearrange("o p f -> p (o f)")).then_inc(w_loaded[q], 16)
                sp.dma_start(k.ew2[:, q, :, :], k.in_ew2[bass.ds(e, 1)].rearrange("o (b p) d -> p (o b) d", p=P)
                             ).then_inc(w_loaded[q], 16)
                sp.dma_start(k.eb1[:, q, :], k.in_eb1[bass.ds(e, 1)].rearrange("o p b -> p (o b)")).then_inc(w_loaded[q], 16)
            load(0, 0)
            load(1, 1)
            with sp.Fori(1, E // 2) as pair:
                for q in (0, 1):
                    sp.wait_ge(y_ready, 2 + C * (2 * pair + q - 1))
                    load(2 * pair + q, q)
            for c in range(C):
                sp.wait_ge(y_added, 8 + 4 * C * (E - 1) + 4 * (c + 1))
                sp.dma_start(k.out[TC * P * c:TC * P * (c + 1), :].rearrange("(t p) d -> p t d", p=P),
                             k.x[:, TC * c:TC * (c + 1), :]).then_inc(stored, 16)
            sp.wait_ge(stored, 16 * C)

        @block.tensor
        def _(pe):
            def up(e, q, c):
                n = e * C + c
                if c == 0:
                    pe.wait_ge(w_loaded[q], 24 * (e - q) + 48)
                for m in range(HB):
                    pe.wait_ge(act_ready, 4 * n + m + 1)
                    pe.matmul(ub[m][:, :], k.ew1[:, q, m * P:(m + 1) * P], k.xnT[:, c * CW:(c + 1) * CW],
                              start=True, stop=True).then_inc(up_ready, 1)

            def down(e, q, c):
                n = e * C + c
                pe.wait_ge(act_ready, 4 + 4 * n + 4)
                pe.wait_ge(y_added, 4 * n + 4)
                for t in range(TC):
                    for b in range(HB):
                        mm = pe.matmul(yb[c % 2][:, t * P:(t + 1) * P], k.hid[:, c % 2, b, t * P:(t + 1) * P],
                                       k.ew2[:, q, b, :], start=(b == 0), stop=(b == HB - 1))
                mm.then_inc(y_ready, 1)

            pe.sem_inc(y_ready, 2)
            with pe.Fori(0, E // 2) as pair:
                e = 2 * pair
                for q in (0, 1):
                    up(e + q, q, 0)
                    for c in range(1, C):
                        up(e + q, q, c)
                        down(e + q, q, c - 1)
                    down(e + q, q, C - 1)

        @block.scalar
        def _(act):
            act.sem_inc(act_ready, 4)
            with act.Fori(0, E // 2) as pair:
                for q, c in [(q, c) for q in (0, 1) for c in range(C)]:
                    n = (2 * pair + q) * C + c
                    for m in range(HB):
                        act.wait_ge(up_ready, 4 * n + m + 1)
                        if m == 0:
                            act.wait_ge(y_ready, n + 1)
                        act.activation(k.hid[:, c % 2, m, :], ub[m][:, :], ACT.Gelu,
                                       bias=k.eb1[:, q, m:m + 1]).then_inc(act_ready, 1)

        @block.vector
        def _(dve):
            dve.sem_inc(y_added, 8)
            with dve.Fori(0, E) as e:
                for c in range(C):
                    n = e * C + c
                    dve.wait_ge(y_ready, 2 + n + 1)
                    for t in range(TC):
                        i = c * TC + t
                        dve.scalar_tensor_tensor(k.x[:, i, :], yb[c % 2][:, t * P:(t + 1) * P],
                                                 k.wts[:, i, bass.ds(e, 1)], k.x[:, i, :], ALU.mult, ALU.add
                                                 ).then_inc(y_added, 1)


def build(nc, i, out):
    k = Core()
    with ExitStack() as ctx:
        sb = lambda n, shape, dt=F32: ctx.enter_context(nc.sbuf_tensor(n, shape, dt))
        sem = lambda n: ctx.enter_context(nc.semaphore(n))

        k.x = sb("x", [P, T, D])
        k.xnT = sb("xnT", [P, S])
        k.Ka = sb("Ka", [P, H, S], BF16)
        k.Qa = sb("Qa", [P, C * G, HG, CW], BF16)
        ring = sb("ring", [P, 8, CW])
        k.V = sb("V", [P, T, D])
        k.Vst = sb("Vst", [P, T, HG, 32])
        k.ident, k.ident_bf = sb("ident", [P, P]), sb("ident_bf", [P, P], BF16)
        k.mask_qk, k.mask_kq = sb("mask_qk", [P, P], BF16), sb("mask_kq", [P, P], BF16)
        k.stats, k.mv = sb("stats", [P, T, 6]), sb("mv", [P, T, 2])
        k.ve, k.std, k.rstd = sb("ve", [P, T]), sb("std", [P, T]), sb("rstd", [P, T])
        flex = sb("flex", [P, 11 * CW])

        QaF = k.Qa[:, :, :, :].bitcast(F32)
        q_flat = QaF.rearrange("p n j s -> p (n j s)")
        v_flat = k.Vst[:, :, :, :].rearrange("p t j w -> p (t j w)")
        split = lambda ap, a: ap.rearrange("p (a b) -> p a b", a=a)
        k.outT = lambda n: QaF[:, bass.ds(n, 1), 0:2, :].rearrange("p o a b -> p (o a b)")
        k.probs = ring
        k.tables = split(ring[:, :, :].rearrange("p a b -> p (a b)"), 2)
        k.xn = k.V
        k.w_qk = v_flat[:, 0:4 * D].rearrange("p (a b c) -> p a b c", a=2, b=2)
        k.w_v = v_flat[:, 4 * D:5 * D]
        k.latent = v_flat[0:LAT + 1, :].rearrange("p (a b c) -> p a b c", a=2, b=2)
        k.t1, k.t2 = split(flex[:, 0:2 * CW], 2), split(flex[:, 2 * CW:4 * CW], 2)
        k.full, k.rest = split(flex[:, 4 * CW:6 * CW], 2), k.t1
        k.part_buf = flex[:, 6 * CW:9 * CW].bitcast(BF16).rearrange("p (w a s) -> p w a s", w=2, a=NPART)
        k.w1, k.w2 = flex[:, 0:CW], flex[:, CW:2 * CW]
        k.h1, k.h2 = split(flex[:, 2 * CW:6 * CW], HB), split(flex[:, 6 * CW:10 * CW], HB)
        k.w3 = split(flex[:, 10 * CW:11 * CW], HB)
        k.act_g, k.act_1, k.act_2 = (split(q_flat[:, a * 4 * CW:(a + 1) * 4 * CW], HB) for a in range(3))
        k.silu, k.y_tmp = split(q_flat[:, 12 * CW:14 * CW], 2), split(q_flat[:, 14 * CW:15 * CW], TC)
        k.hid = q_flat[:, 0:8 * CW].rearrange("p (a b c) -> p a b c", a=2, b=HB)
        k.ew1 = split(q_flat[:, 8 * CW:10 * CW], 2)
        k.ew2 = q_flat[:, 10 * CW:12 * CW].rearrange("p (a b c) -> p a b c", a=2, b=HB)

        k.negsplit, k.shiftT = sb("negsplit", [P, TC, 32], BF16), sb("shiftT", [P, TC * 32], BF16)
        k.maxp, k.maxu = sb("maxp", [P, C, TC, HG]), sb("maxu", [P, TC, HG])
        k.inv, k.heads, k.headsT = sb("inv", [P, 2, H]), ring[:, 0, :].rearrange("p (a b) -> p a b", a=4)[:, 0:2], \
            ring[:, 1, :].rearrange("p (a b) -> p a b", a=4)[:, 0:2]
        k.w_out = [sb("w_out0", [P, D]), sb("w_out1", [P, D])]
        k.s1, k.s2, k.sh1, k.sh2 = (sb(n, [P, HB]) for n in ("s1", "s2", "sh1", "sh2"))
        k.s3_rows, k.bo_rows = sb("s3_rows", [P, D]), sb("bo_rows", [P, D])
        k.b_down, k.b_kr = sb("b_down", [P, 1]), sb("b_kr", [P, 2])
        latw = split(flex[:, 9 * CW:11 * CW], 8)
        k.w_down, k.w_kr = latw[:, 0, :], latw[:, 1:3, :]
        k.w_qr, k.w_up = latw[0:LAT + 1, 3:5, :], latw[0:LAT + 1, 5:8, :]
        k.gate_w, k.gate_b_rows = sb("gate_w", [P, E]), sb("gate_b_rows", [P, E])
        k.eb1, k.b2 = sb("eb1", [P, 2, HB]), sb("b2", [E, D])
        k.g, k.top, k.top_i = (split(flex[:, n * T * E:(n + 1) * T * E], T) for n in range(3))
        k.top_i = k.top_i.bitcast(U32)
        k.top_f, k.g_diff, k.g_exp = sb("top_f", [P, T, 2]), sb("g_diff", [P, T]), sb("g_exp", [P, T])
        k.g_sum, k.p1, k.p2 = sb("g_sum", [P, T]), sb("p1", [P, T]), sb("p2", [P, T])
        k.hit, k.wts, k.wtsT = (split(q_flat[:, 12 * CW:12 * CW + 2 * T * E], 2).rearrange("p r (t e) -> p r t e", t=T),
                                sb("wts", [P, T, E]), q_flat[0:E, 13 * CW:17 * CW])
        k.expert_i, k.expert = sb("expert_i", [P, E], mybir.dt.int32), sb("expert", [P, E])

        k.bank = [ctx.enter_context(nc.psum_tensor(f"bank{n}", [P, CW], F32)) for n in range(8)]

        k.parts = [nc.dram_tensor(f"{n}_parts", [NPART, D, S], BF16).ap() for n in ("q", "k")]
        k.shift_dram = nc.dram_tensor("shift_rows", [P, TC * 32], BF16).ap()

        k.weights_loaded, k.tables_loaded, k.ones_ready = sem("weights_loaded"), sem("tables_loaded"), sem("ones_ready")
        k.zeros_ready = sem("zeros_ready")
        k.laid_out = [sem("laid_out0"), sem("laid_out1")]
        k.next_loaded = [sem("ffn_weights_loaded"), sem("gate_weights_loaded")]

        rows = lambda ap: ap.rearrange("(o n) -> o n", o=1).partition_broadcast(P)
        k.in_x, k.out, k.in_ew1, k.in_ew2, k.in_eb1 = i["x"], out, i["ew1"], i["ew2"], i["eb1"]
        k.in_tables0, k.in_tables1 = i["tables0"], i["tables1"]
        k.first_loads = [
            (k.w_qk, i["w_qk"].rearrange("w r p o -> p w r o")), (k.w_v, i["w_v"]),
            (k.w_out[0][:, :], i["w_out0"]), (k.w_out[1][:, :], i["w_out1"]),
            (k.s1[:, :], i["s1"]), (k.s2[:, :], i["s2"]), (k.sh1[:, :], i["sh1"]), (k.sh2[:, :], i["sh2"]),
            (k.b_down[:, :], i["b_down"]), (k.b_kr[:, :], i["b_kr"]),
            (k.s3_rows[:, :], i["s3"].partition_broadcast(P)), (k.bo_rows[:, :], i["bo"].partition_broadcast(P)),
        ]
        k.latent_loads = [
            (k.w_down[:, :], i["w_down"]), (k.w_kr[:, :, :], i["w_kr"].rearrange("r p o -> p r o")),
            (k.w_qr[:, :, :], i["w_qr"].rearrange("r p o -> p r o")), (k.w_up[:, :, :], i["w_up"].rearrange("r p o -> p r o")),
        ]
        by_block = lambda ap: ap.rearrange("(b p) o -> p b o", p=P)
        k.attention_loads = [
            [(k.w1, i["w1"]), (k.w2, i["w2"]), (k.h1, by_block(i["h1"])), (k.h2, by_block(i["h2"])), (k.w3, by_block(i["w3"]))],
            [(k.gate_w[:, :], i["gate_w"]), (k.gate_b_rows[:, :], i["gate_b"].partition_broadcast(P)),
             (k.b2[:, :], i["b2"])],
        ]

        norm_phase(nc, k, "norm0", first=True)
        project_phase(nc, k, 0)
        attention_phase(nc, k, 0)
        output_phase(nc, k, 0)
        norm_phase(nc, k, "norm1")
        ffn_phase(nc, k)
        norm_phase(nc, k, "norm2", loads=k.latent_loads)
        project_phase(nc, k, 1)
        attention_phase(nc, k, 1)
        output_phase(nc, k, 1)
        norm_phase(nc, k, "norm3")
        gate_phase(nc, k)
        experts_phase(nc, k)


def rotary_tables():
    pos = np.arange(S, dtype=np.float32)
    half = HD // 2
    f0 = (np.float32(1.0) / np.float32(10000.0) ** (np.arange(half, dtype=np.float32) / np.float32(half))).astype(np.float32)
    ids = np.arange(D // 2, dtype=np.float32)
    f1 = (np.float32(10000.0) ** (np.float32(-2.0) * ids) / np.float32(D // 2)).astype(np.float32)
    row = np.arange(D)
    a0 = f0[row % HD % half][:, None] * pos[None, :]
    s0 = np.where(row % HD < half, -1.0, 1.0).astype(np.float32)
    a1 = f1[row // 2][:, None] * pos[None, :]
    s1 = np.where(row % 2 == 0, -1.0, 1.0).astype(np.float32)
    return [np.stack([np.cos(a), np.sin(a) * s[:, None]]).astype(np.float32) for a, s in ((a0, s0), (a1, s1))]


def kernel(**inputs):
    import concourse.bacc as bacc
    from concourse.bass_utils import run_bass_kernel_spmd

    a = {n: np.asarray(v) for n, v in inputs.items()}
    swap0 = lambda w: w.reshape(-1, H, 2, HD // 2)[:, :, ::-1, :].reshape(-1, D)
    swap1 = lambda w: w.reshape(-1, D // 2, 2)[:, :, ::-1].reshape(-1, D)
    with_bias = lambda w, b: np.concatenate([w, b[None, :]], 0)
    columns = lambda s: s.reshape(-1, P).T
    wq, wk, wv = (a["L0_attn_w_qkv"][D * n:D * (n + 1)].T for n in range(3))
    wqr = with_bias(a["L1_attn_Wq_r_w"], a["L1_attn_Wq_r_b"])
    wkr, bkr = a["L1_attn_Wk_r_w"], a["L1_attn_Wk_r_b"]
    tables = rotary_tables()
    arrays = {
        "x": a["L0_attn_x"].reshape(S, D),
        "tables0": tables[0], "tables1": tables[1],
        "w_qk": np.stack([np.stack([w, swap0(w)]) for w in (wq, wk)]), "w_v": wv,
        "w_out0": a["L0_attn_w_out"].T, "w_out1": a["L1_attn_Wo_w"],
        "s1": columns(a["L0_ffn_w1_s"]), "s2": columns(a["L0_ffn_w2_s"]),
        "sh1": columns(a["L0_ffn_h1_s"]), "sh2": columns(a["L0_ffn_h2_s"]),
        "w1": a["L0_ffn_w1_w"].T, "w2": a["L0_ffn_w2_w"].T, "h1": a["L0_ffn_h1_w"].T, "h2": a["L0_ffn_h2_w"].T,
        "w3": a["L0_ffn_w3_w"].T, "s3": a["L0_ffn_w3_s"],
        "w_down": np.concatenate([a["L1_attn_Wd_q_w"], a["L1_attn_Wd_kv_w"]], 1),
        "b_down": np.concatenate([a["L1_attn_Wd_q_b"], a["L1_attn_Wd_kv_b"]])[:, None],
        "w_qr": np.stack([wqr, swap1(wqr)]),
        "w_kr": np.stack([wkr, swap1(wkr)]), "b_kr": np.concatenate([bkr[None], swap1(bkr[None])]).T,
        "w_up": np.stack([with_bias(a[f"L1_attn_{n}_w"], a[f"L1_attn_{n}_b"]) for n in ("Wu_q", "Wu_k", "Wu_v")]),
        "bo": a["L1_attn_Wo_b"],
        "gate_w": a["L1_ffn_gate_w"].T, "gate_b": a["L1_ffn_gate_b"],
        "eb1": a["L1_ffn_b1"].reshape(E, HB, P).transpose(0, 2, 1), "b2": a["L1_ffn_b2"],
        "ew1": a["L1_ffn_w1"], "ew2": a["L1_ffn_w2"],
    }
    arrays = {f"in_{n}": np.ascontiguousarray(v) for n, v in arrays.items()}
    nc = bacc.Bacc("TRN2", target_bir_lowering=False, num_devices=1)
    ins = {n[3:]: nc.dram_tensor(n, v.shape, mybir.dt.from_np(v.dtype), kind="ExternalInput").ap()
           for n, v in arrays.items()}
    out = nc.dram_tensor("out", (S, D), F32, kind="ExternalOutput").ap()
    build(nc, ins, out)
    result = run_bass_kernel_spmd(nc, [arrays], core_ids=[0])
    return result.results[0]["out"].reshape(1, S, D)
```
